# Optimizing a Trainium2 kernel written in Bass

```python
import numpy as np
import jax
import jax.numpy as jnp

def _softmax(x, axis=-1):
    return jax.nn.softmax(x, axis=axis)

def _gelu(x):
    return jax.nn.gelu(x, approximate=True)

def _silu(x):
    return jax.nn.silu(x)

def _sigmoid(x):
    return jax.nn.sigmoid(x)

def _layernorm(x, axis=-1, eps=1e-05):
    m = jnp.mean(x, axis=axis, keepdims=True)
    v = jnp.var(x, axis=axis, keepdims=True)
    return (x - m) / jnp.sqrt(v + eps)

def _scatter_add(tgt, idx, src, axis=0):
    return tgt.at[idx].add(src)

def _segment_sum(src, seg, n):
    return jax.ops.segment_sum(src, seg, n)
kernel_name = 'mk_prb_d1_jaxref_r4_89203e'

def setup_inputs(seed: int=0):
    np.random.seed(seed)
    _w = jnp.asarray

    def _L0_attn_setup():
        import jax, jax.numpy as jnp
        import numpy as np
        B, T, D, P, ALPHA, PR = (4, 1024, 256, 128, 4, 64)
        key = jax.random.key(seed)
        ks = jax.random.split(key, 9)
        g = lambda k, shape, scale: jax.random.normal(k, shape, jnp.float32) * scale
        return {'x': jax.random.normal(ks[0], (B, T, D), jnp.float32), 'W_toP': g(ks[1], (D, P), D ** (-0.5)), 'W_U': g(ks[2], (D, P, ALPHA), D ** (-0.5)), 'W_F': g(ks[3], (D, P), D ** (-0.5)), 'W_V': g(ks[4], (P, ALPHA), 1.0), 'W_lam': g(ks[5], (P, PR), P ** (-0.5)), 'B_mat': g(ks[6], (P, PR), P ** (-0.5)), 'C_mat': g(ks[7], (PR, P), PR ** (-0.5)), 'W_fromP': g(ks[8], (P, D), P ** (-0.5))}
    _L0_attn_in = _L0_attn_setup()

    def _L0_ffn_setup():
        import jax, jax.numpy as jnp
        import numpy as np

        def _bitlinear(x, w_latent):
            scale = jax.lax.stop_gradient(jnp.clip(jnp.mean(jnp.abs(w_latent), axis=1, keepdims=True), 1e-05, None))
            tern = jnp.clip(jnp.round(w_latent / scale), -1.0, 1.0)
            w = w_latent + jax.lax.stop_gradient(tern - w_latent)
            return x @ (w * scale).T
        key = jax.random.key(seed)
        ks = jax.random.split(key, 6)
        dim, hidden, rank = (256, 1024, 16)
        B, S = (4, 1024)
        x = jax.random.normal(ks[0], (B, S, dim), dtype=jnp.float32)
        w_fc = 0.02 * jax.random.normal(ks[1], (hidden, dim), dtype=jnp.float32)
        w_proj = 0.02 * jax.random.normal(ks[2], (dim, hidden), dtype=jnp.float32)
        u = 0.02 * jax.random.normal(ks[3], (hidden, rank), dtype=jnp.float32)
        v = 0.02 * jax.random.normal(ks[4], (rank, dim), dtype=jnp.float32)
        fast_b = jax.random.normal(ks[5], (rank, rank), dtype=jnp.float32)
        gate = jnp.float32(0.05)
        return {'x': x, 'fast_b': fast_b, 'w_fc': w_fc, 'w_proj': w_proj, 'u': u, 'v': v, 'gate': gate}
    _L0_ffn_in = _L0_ffn_setup()
    _d = {'L0_attn_x': _L0_attn_in['x'], 'L0_attn_W_toP': _L0_attn_in['W_toP'], 'L0_attn_W_U': _L0_attn_in['W_U'], 'L0_attn_W_F': _L0_attn_in['W_F'], 'L0_attn_W_V': _L0_attn_in['W_V'], 'L0_attn_W_lam': _L0_attn_in['W_lam'], 'L0_attn_B_mat': _L0_attn_in['B_mat'], 'L0_attn_C_mat': _L0_attn_in['C_mat'], 'L0_attn_W_fromP': _L0_attn_in['W_fromP'], 'L0_ffn_fast_b': _L0_ffn_in['fast_b'], 'L0_ffn_w_fc': _L0_ffn_in['w_fc'], 'L0_ffn_w_proj': _L0_ffn_in['w_proj'], 'L0_ffn_u': _L0_ffn_in['u'], 'L0_ffn_v': _L0_ffn_in['v'], 'L0_ffn_gate': _L0_ffn_in['gate']}
    _x0 = _d['L0_attn_x']
    _d['L0_attn_x'] = jax.random.normal(jax.random.fold_in(jax.random.key(seed), 1), (16, 1024, 256), dtype=_x0.dtype)
    del _x0
    return _d

def reference(L0_attn_x, L0_attn_W_toP, L0_attn_W_U, L0_attn_W_F, L0_attn_W_V, L0_attn_W_lam, L0_attn_B_mat, L0_attn_C_mat, L0_attn_W_fromP, L0_ffn_fast_b, L0_ffn_w_fc, L0_ffn_w_proj, L0_ffn_u, L0_ffn_v, L0_ffn_gate):

    def _L0_attn_ref(x, W_toP, W_U, W_F, W_V, W_lam, B_mat, C_mat, W_fromP):
        import jax, jax.numpy as jnp
        import numpy as np
        B, T, D, P, ALPHA, PR = (4, 1024, 256, 128, 4, 64)
        pre = jnp.einsum('btd,dp->btp', x, W_toP)
        U = jnp.einsum('btd,dpa->btpa', x, W_U)
        Fg = jax.nn.sigmoid(jnp.einsum('btd,dp->btp', x, W_F))
        Y = U * W_V
        t = Y.sum(-1) + pre
        lam = jax.nn.sigmoid(jnp.einsum('btp,pr->btr', Fg, W_lam))
        u_in = jnp.einsum('btp,pr->btr', t, B_mat)

        def step(s, inp):
            l, u = inp
            s = l * s + u
            return (s, s)
        s0 = jnp.zeros((x.shape[0], PR), x.dtype)
        _, s_seq = jax.lax.scan(step, s0, (lam.transpose(1, 0, 2), u_in.transpose(1, 0, 2)))
        s_seq = s_seq.transpose(1, 0, 2)
        t_tilde = t + jnp.einsum('btr,rp->btp', s_seq, C_mat)
        h = jnp.einsum('btp,pd->btd', t_tilde, W_fromP)
        return h

    def _L0_ffn_ref(x, fast_b, w_fc, w_proj, u, v, gate):
        import jax, jax.numpy as jnp
        import numpy as np

        def _bitlinear(x, w_latent):
            scale = jax.lax.stop_gradient(jnp.clip(jnp.mean(jnp.abs(w_latent), axis=1, keepdims=True), 1e-05, None))
            tern = jnp.clip(jnp.round(w_latent / scale), -1.0, 1.0)
            w = w_latent + jax.lax.stop_gradient(tern - w_latent)
            return x @ (w * scale).T
        h = _bitlinear(x, w_fc) + gate * (x @ v.T @ fast_b.T @ u.T)
        r = jnp.maximum(h, 0.0)
        return _bitlinear(r * r, w_proj)
    x = L0_attn_x
    xn = _layernorm(x, axis=-1)
    x = x + _L0_attn_ref(xn, L0_attn_W_toP, L0_attn_W_U, L0_attn_W_F, L0_attn_W_V, L0_attn_W_lam, L0_attn_B_mat, L0_attn_C_mat, L0_attn_W_fromP) + _L0_ffn_ref(xn, L0_ffn_fast_b, L0_ffn_w_fc, L0_ffn_w_proj, L0_ffn_u, L0_ffn_v, L0_ffn_gate)
    return x

_drawn_inputs = setup_inputs


def setup_inputs(seed=0):
    import zlib

    import numpy as np

    out = dict(_drawn_inputs(seed))
    spreads = {}
    factors = {'L0_ffn_fast_b': 8.0,
     'L0_ffn_w_fc': 6.575,
     'L0_ffn_w_proj': 5.217,
     'L0_ffn_u': 8.0,
     'L0_ffn_v': 8.0,
     'L0_attn_W_F': 8.0,
     'L0_attn_W_lam': 3.539}
    for name, (base, spread) in spreads.items():
        noise = np.random.default_rng([zlib.crc32(name.encode()), seed]).standard_normal(out[name].shape)
        drawn = base * np.exp(spread * noise) if base else spread * noise
        out[name] = jnp.asarray(drawn.astype(out[name].dtype))
    for name, factor in factors.items():
        out[name] = (out[name] * factor).astype(out[name].dtype)
    return out
```

```python
from contextlib import ExitStack

import concourse.bass as bass
from concourse import mybir

F32 = mybir.dt.float32
F32R = mybir.dt.float32r
I32 = mybir.dt.int32
ALU = mybir.AluOpType
ACT = mybir.ActivationFunctionType
AX = mybir.AxisListType

P = 128
TOK = 512
CH = TOK // P
UNROLL = 4
LAG = 2
QR = 4
EPS = 1e-5
NEWTON = 3
POOL_STEPS = 4 + 4 * NEWTON - 1
RSQRT_BITS = float(0x5F3759DF)


def at(tile, per, more):
    value = tile * per + more
    return max(value, 0) if isinstance(value, int) else value


def ring_dma(tile, slot, ring):
    return at(tile, 16 // ring, 16 - slot * 16 // ring)


def build(nc, x, W_toP, W_U, W_F, W_V, W_lam, B_mat, C_mat, W_fromP, fast_b, w_fc, w_proj, u, v, gate, out):
    NB, T, D = x.shape
    HID = w_fc.shape[0]
    PR = W_lam.shape[1]
    R = fast_b.shape[0]
    AL = W_V.shape[1]
    NT = NB * T // TOK
    TPS = T // TOK
    KD = D // P
    H = HID // P
    assert (KD, H, CH, TPS) == (2, 8, 4, 2) and PR == 64 and 4 * R == P - PR and NT % UNROLL == 0

    x_t = x.rearrange("b t d -> (b t) d").rearrange("(n c p) d -> n p c d", c=CH, p=P)
    out_t = out.rearrange("b t d -> (b t) d").rearrange("(n c p) d -> n p c d", c=CH, p=P)

    with ExitStack() as ctx:
        def sb(name, shape, dt=F32):
            return ctx.enter_context(nc.sbuf_tensor(name, shape, dt))

        def sem(name):
            return ctx.enter_context(nc.semaphore(name))

        wfc_nat = sb("wfc_nat", [P, H, D])
        wpj_nat = sb("wpj_nat", [P, KD, HID])
        wtop_nat = sb("wtop_nat", [P, KD, P])
        wu_nat = sb("wu_nat", [P, KD, P * AL])
        wv_all = sb("wv_all", [P, P * AL])
        wf_nat = sb("wf_nat", [P, KD, P])
        wlam_nat = sb("wlam_nat", [P, PR])
        b_nat = sb("b_nat", [P, PR])
        cc_nat = sb("cc_nat", [P, P])
        wfrom_nat = sb("wfrom_nat", [P, D])
        fb_nat = sb("fb_nat", [R, R])
        u_nat = sb("u_nat", [P, H, R])
        v_nat = sb("v_nat", [R, D])
        gate_all = sb("gate_all", [P, 1])
        ident = sb("ident", [P, P])

        tern1 = sb("tern1", [P, KD, HID], F32R)
        tern2 = sb("tern2", [P, H, D], F32R)
        low_st = sb("low_st", [P, HID], F32R)
        wt_h = sb("wt_h", [P, KD, P], F32R)
        wt_l = sb("wt_l", [P, KD, P], F32R)
        wf_h = sb("wf_h", [P, KD, P], F32R)
        wf_l = sb("wf_l", [P, KD, P], F32R)
        uz_h = sb("uz_h", [P, KD, P], F32R)
        uz_l = sb("uz_l", [P, KD, P], F32R)
        wlam_h = sb("wlam_h", [P, PR], F32R)
        wlam_l = sb("wlam_l", [P, PR], F32R)
        cc_h = sb("cc_h", [P, P], F32R)
        cc_l = sb("cc_l", [P, P], F32R)
        wfrom_h = sb("wfrom_h", [P, D], F32R)
        wfrom_l = sb("wfrom_l", [P, D], F32R)
        s1 = sb("s1", [P, H])
        s2 = sb("s2", [P, KD])

        s1_half = sb("s1_half", [P, H])
        s1_neg = sb("s1_neg", [P, H])
        s2_half = sb("s2_half", [P, KD])
        s2_neg = sb("s2_neg", [P, KD])
        s2_inv = sb("s2_inv", [P, KD])
        s1_inv = sb("s1_inv", [P, H])
        gate_s1 = sb("gate_s1", [P, H])
        t1_nat = sb("t1_nat", [P, H, D])
        t2_nat = sb("t2_nat", [P, KD, HID])
        wt_nat = sb("wt_nat", [P, KD, P])
        wtT = sb("wtT", [P, D])
        uz_nat = sb("uz_nat", [P, KD, P])
        wfromT = sb("wfromT", [P, KD, P])
        uT = sb("uT", [R, HID])
        low_nat = sb("low_nat", [P, H, R])
        low_hr = sb("low_hr", [P, H, R], F32R)
        low_rep = sb("low_rep", [P, H, P])

        xbuf = sb("xbuf", [P, UNROLL, CH, D])
        stats = sb("stats", [P, CH, 6])
        mean = sb("mean", [P, CH])
        m_dif = sb("m_dif", [P, CH])
        var_eps = sb("var_eps", [P, CH])
        var_half = sb("var_half", [P, CH])
        c_half, c_quarter, c_minus_half, c_three_half, c_count, c_eps = (
            sb(f"c_{n}", [P, CH]) for n in ("half", "quarter", "minus_half", "three_half", "count", "eps"))
        rstd = sb("rstd", [P, CH])
        newton = sb("newton", [P, CH])
        xn = sb("xn", [P, CH, D])
        xT_h = sb("xT_h", [P, 2, KD, TOK], F32R)
        xT_l = sb("xT_l", [P, 2, KD, TOK], F32R)
        fg = sb("fg", [P, TOK])
        fg_h = sb("fg_h", [P, TOK], F32R)
        fg_l = sb("fg_l", [P, TOK], F32R)
        lam = sb("lam", [PR, TOK])
        s_seq = sb("s_seq", [PR, 2, TOK])
        s_st = sb("s_st", [P, TOK], F32R)
        z_st = sb("z_st", [P, 2, TOK], F32R)
        t_h = sb("t_h", [P, TOK], F32R)
        t_l = sb("t_l", [P, TOK], F32R)
        r_buf = sb("r_buf", [P, 2, TOK])
        q_buf = sb("q_buf", [P, QR, TOK])
        q_h = sb("q_h", [P, QR, TOK], F32R)
        q_l = sb("q_l", [P, QR, TOK], F32R)
        yT = sb("yT", [P, KD, TOK])
        obuf = sb("obuf", [P, 2, CH, D])

        bank = [ctx.enter_context(nc.psum_tensor(f"bank{n}", [P, TOK], F32)) for n in range(8)]
        p_bank = bank[0:2]
        y_bank = bank[2:4]
        m_bank = bank[4:8]

        w_loaded = {n: sem(f"w_loaded_{n}") for n in ("fc", "proj", "top", "u", "small")}
        x_loaded = [sem(f"x_loaded{n}") for n in range(UNROLL)]
        stored = [sem(f"stored{n}") for n in range(2)]
        ident_ready = sem("ident_ready")
        zeros_ready = sem("zeros_ready")
        prep_pe = sem("prep_pe")
        prep_out = sem("prep_out")
        prep_dve = sem("prep_dve")
        t1_ready = sem("t1_ready")
        t2_ready = sem("t2_ready")
        wt_ready = sem("wt_ready")
        low_ready = sem("low_ready")
        weights_ready = sem("weights_ready")
        bn_done = sem("bn_done")
        var_done = sem("var_done")
        guess_done = sem("guess_done")
        pool_steps = sem("pool_steps")
        rstd_done = sem("rstd_done")
        xn_done = sem("xn_done")
        xT_ready = sem("xT_ready")
        xTh_done = sem("xTh_done")
        xTl_done = sem("xTl_done")
        f_ready = sem("f_ready")
        fg_done = sem("fg_done")
        fgh_done = sem("fgh_done")
        fgl_done = sem("fgl_done")
        uz_ready = sem("uz_ready")
        zh_done = sem("zh_done")
        zl_done = sem("zl_done")
        laml_ready = sem("laml_ready")
        lam_done = sem("lam_done")
        scan_done = sem("scan_done")
        sh_done = sem("sh_done")
        sl_done = sem("sl_done")
        t_ready = sem("t_ready")
        th_done = sem("th_done")
        tl_done = sem("tl_done")
        p_ready = sem("p_ready")
        r_done = sem("r_done")
        q_done = sem("q_done")
        qh_done = sem("qh_done")
        ql_done = sem("ql_done")
        q_used = sem("q_used")
        y_done = sem("y_done")
        oT_ready = sem("oT_ready")
        added = sem("added")

        PREP_BANKS = 17

        block = ctx.enter_context(nc.Block())

        def run_tiles(eng, tile_steps):
            for i in range(UNROLL):
                tile_steps(i, i)
            with eng.Fori(1, NT // UNROLL - 1) as turn:
                for k in range(UNROLL):
                    tile_steps(turn * UNROLL + k, k)
            for k in range(UNROLL):
                tile_steps(NT - UNROLL + k, k)

        def is_tile(i, n):
            return isinstance(i, int) and i == n

        @block.sync
        def _(sp):
            sp.dma_start(xbuf[:, 0, :, :], x_t[0]).then_inc(x_loaded[0], 16)
            sp.dma_start(wfc_nat[:, :, :], w_fc.rearrange("(h p) d -> p h d", p=P)).then_inc(w_loaded["fc"], 16)
            sp.dma_start(wpj_nat[:, :, :], w_proj.rearrange("(g p) h -> p g h", p=P)).then_inc(w_loaded["proj"], 16)
            sp.dma_start(xbuf[:, 1, :, :], x_t[1]).then_inc(x_loaded[1], 16)
            sp.dma_start(xbuf[:, 2, :, :], x_t[2]).then_inc(x_loaded[2], 16)
            sp.dma_start(xbuf[:, 3, :, :], x_t[3]).then_inc(x_loaded[3], 16)

            def tile_steps(i, k):
                if is_tile(i, 0):
                    return
                sp.wait_ge(added, at(i, 2, 0))
                sp.dma_start(out_t[bass.ds(i - 1, 1)].rearrange("n p c d -> p (n c) d"),
                             obuf[:, (k - 1) % 2, :, :]).then_inc(stored[(k - 1) % 2], 16)
                if isinstance(i, int) and i + 3 >= NT:
                    return
                sp.dma_start(xbuf[:, (k + 3) % UNROLL, :, :],
                             x_t[bass.ds(i + 3, 1)].rearrange("n p c d -> p (n c) d")
                             ).then_inc(x_loaded[(k + 3) % UNROLL], 16)

            run_tiles(sp, tile_steps)
            sp.wait_ge(added, 2 * NT)
            sp.dma_start(out_t[NT - 1], obuf[:, (NT - 1) % 2, :, :]).then_inc(stored[(NT - 1) % 2], 16)
            for n in range(2):
                sp.wait_ge(stored[n], 16 * NT // 2)

        @block.gpsimd
        def _(pool):
            pool.memset(ident[:, :], 0.0).then_inc(ident_ready, 1)
            pool.wait_ge(ident_ready, 1)
            pool.affine_select(out=ident[:, :], in_=ident[:, :], compare_op=ALU.not_equal, fill=1.0,
                               base=0, pattern=[[-1, P]], channel_multiplier=1).then_inc(ident_ready, 1)
            for tile, value in ((c_half, 0.5), (c_quarter, 0.25), (c_minus_half, -0.5), (c_three_half, 1.5),
                                (c_count, 1.0 / D), (c_eps, EPS)):
                ins = pool.memset(tile[:, :], value)
            ins.then_inc(ident_ready, 1)
            pool.wait_ge(ident_ready, 3)
            pool.memset(low_rep[:, :, 0:PR], 0.0).then_inc(zeros_ready, 1)
            pool.memset(z_st[0:PR, :, :].bitcast(F32), 0.0).then_inc(zeros_ready, 1)

            def moments_of(i):
                steps = [0]

                def link(ins):
                    steps[0] += 1
                    ins.then_inc(pool_steps, 1)
                    pool.wait_ge(pool_steps, at(i, POOL_STEPS, steps[0]))

                tt = pool.tensor_tensor
                pool.wait_ge(bn_done, at(i, CH, CH))
                pool.wait_ge(xn_done, at(i, CH, 0))
                tt(mean[:, :], stats[:, :, 1], stats[:, :, 4], ALU.add)
                tt(m_dif[:, :], stats[:, :, 1], stats[:, :, 4], ALU.subtract)
                link(tt(var_eps[:, :], stats[:, :, 2], stats[:, :, 5], ALU.add))
                tt(mean[:, :], mean[:, :], c_half[:, :], ALU.mult)
                tt(m_dif[:, :], m_dif[:, :], m_dif[:, :], ALU.mult)
                link(tt(var_eps[:, :], var_eps[:, :], c_count[:, :], ALU.mult))
                tt(m_dif[:, :], m_dif[:, :], c_quarter[:, :], ALU.mult)
                link(tt(var_eps[:, :], var_eps[:, :], c_eps[:, :], ALU.add))
                link(tt(var_eps[:, :], var_eps[:, :], m_dif[:, :], ALU.add))
                tt(var_half[:, :], var_eps[:, :], c_minus_half[:, :], ALU.mult).then_inc(var_done, 1)
                pool.wait_ge(guess_done, at(i, 1, 1))
                for n in range(NEWTON):
                    link(tt(newton[:, :], rstd[:, :], rstd[:, :], ALU.mult))
                    link(tt(newton[:, :], newton[:, :], var_half[:, :], ALU.mult))
                    link(tt(newton[:, :], newton[:, :], c_three_half[:, :], ALU.add))
                    ins = tt(rstd[:, :], rstd[:, :], newton[:, :], ALU.mult)
                    if n < NEWTON - 1:
                        link(ins)
                    else:
                        ins.then_inc(rstd_done, 1)
                assert steps[0] == POOL_STEPS

            def fg_low(i):
                pool.wait_ge(fgh_done, at(i, 1, 1))
                pool.wait_ge(laml_ready, at(i, 1, 0))
                pool.tensor_tensor(fg_l[:, :], fg[:, :], fg_h[:, :], ALU.subtract).then_inc(fgl_done, 1)

            moments_of(0)
            moments_of(1)
            fg_low(0)

            def tile_steps(i, k):
                if not (isinstance(i, int) and i + 2 >= NT):
                    moments_of(i + 2)
                if not is_tile(i, NT - 1):
                    fg_low(i + 1)

            run_tiles(pool, tile_steps)

        @block.scalar
        def _(act):
            act.dma_start(wtop_nat[:, :, :], W_toP.rearrange("(k p) n -> p k n", p=P)).then_inc(w_loaded["top"], 16)
            act.dma_start(wu_nat[:, :, :], W_U.rearrange("(k p) n a -> p k (n a)", p=P)).then_inc(w_loaded["u"], 16)
            act.dma_start(wv_all[:, :], W_V.rearrange("n a -> (n a)").rearrange("(o m) -> o m", o=1)
                          .broadcast_to([P, P * AL])).then_inc(w_loaded["small"], 16)
            act.dma_start(wf_nat[:, :, :], W_F.rearrange("(k p) n -> p k n", p=P)).then_inc(w_loaded["small"], 16)
            act.dma_start(wlam_nat[:, :], W_lam).then_inc(w_loaded["small"], 16)
            act.dma_start(b_nat[:, :], B_mat).then_inc(w_loaded["small"], 16)
            act.dma_start(cc_nat[0:PR, :], C_mat).then_inc(w_loaded["small"], 16)
            act.dma_start(cc_nat[PR:P, :], C_mat).then_inc(w_loaded["small"], 16)
            act.dma_start(wfrom_nat[:, :], W_fromP).then_inc(w_loaded["small"], 16)
            act.dma_start(fb_nat[:, :], fast_b).then_inc(w_loaded["small"], 16)
            act.dma_start(u_nat[:, :, :], u.rearrange("(h p) r -> p h r", p=P)).then_inc(w_loaded["small"], 16)
            act.dma_start(v_nat[:, :], v).then_inc(w_loaded["small"], 16)
            act.dma_start(gate_all[:, :], gate.broadcast_to([P, 1])).then_inc(w_loaded["small"], 16)

            def t_high(i):
                act.wait_ge(t_ready, at(i, 1, 1))
                act.wait_ge(q_used, at(i, H, 1 - H))
                act.activation(t_h[:, :], m_bank[1][:, :], ACT.Copy).then_inc(th_done, 1)

            def xT_high(i, k):
                for half in range(KD):
                    act.wait_ge(xT_ready, at(i, KD, half + 1))
                    act.wait_ge(p_ready, at(i, H, -H))
                    act.activation(xT_h[:, k % 2, half, :], m_bank[half][:, :], ACT.Copy).then_inc(xTh_done, 1)

            def gates(i):
                act.wait_ge(f_ready, at(i, 1, 1))
                act.wait_ge(fgl_done, at(i, 1, 0))
                act.activation(fg[:, :], m_bank[2][:, :], ACT.Sigmoid).then_inc(fg_done, 1)
                act.wait_ge(laml_ready, at(i, 1, 0))
                act.activation(fg_h[:, :], m_bank[2][:, :], ACT.Sigmoid).then_inc(fgh_done, 1)

            def z_high(i, k):
                act.wait_ge(uz_ready, at(i, 1, 1))
                act.wait_ge(p_ready, at(i, H, -H))
                act.activation(z_st[PR:P, k % 2, :], m_bank[0][PR:P, :], ACT.Copy).then_inc(zh_done, 1)

            def decay(i):
                act.wait_ge(laml_ready, at(i, 1, 1))
                act.wait_ge(scan_done, at(i, 1, 0))
                act.activation(lam[:, :], m_bank[2][0:PR, :], ACT.Sigmoid).then_inc(lam_done, 1)

            def relu(i, h):
                act.wait_ge(p_ready, at(i, H, h + 1))
                act.wait_ge(q_done, at(i, H, h - 1))
                act.activation(r_buf[:, h % 2, :], p_bank[h % 2][:, :], ACT.Relu,
                               scale=s1[:, h:h + 1]).then_inc(r_done, 1)

            def square(i, h):
                act.wait_ge(r_done, at(i, H, h + 1))
                act.wait_ge(ql_done, at(i, H, h + 1 - QR))
                act.activation(q_buf[:, h % QR, :], r_buf[:, h % 2, :], ACT.Square).then_inc(q_done, 1)

            def y_scaled(i):
                act.wait_ge(q_used, at(i, H, H))
                act.wait_ge(oT_ready, at(i, 2, 0))
                for half in range(KD):
                    act.activation(yT[:, half, :], y_bank[half][:, :], ACT.Copy,
                                   scale=s2[:, half:half + 1]).then_inc(y_done, 1)

            xT_high(0, 0)
            act.wait_ge(weights_ready, 1)
            gates(0)
            z_high(0, 0)
            decay(0)

            def tile_steps(i, k):
                last = is_tile(i, NT - 1)
                for h in range(H):
                    if h == 0:
                        t_high(i)
                    relu(i, h)
                    if h == 1 and not last:
                        xT_high(i + 1, k + 1)
                    if h == 2 and not is_tile(i, 0):
                        y_scaled(i - 1)
                    square(i, h)
                    if last:
                        continue
                    if h == 2:
                        gates(i + 1)
                    if h == 3:
                        z_high(i + 1, k + 1)
                    if h == 5:
                        decay(i + 1)

            run_tiles(act, tile_steps)
            y_scaled(NT - 1)

        @block.vector
        def _(dve):
            links = [0]

            def link(ins):
                links[0] += 1
                ins.then_inc(prep_dve, 1)
                dve.wait_ge(prep_dve, links[0])

            def moments(i, k):
                dve.wait_ge(x_loaded[k % UNROLL], ring_dma(i, k % UNROLL, UNROLL))
                dve.wait_ge(var_done, at(i, 1, 0))
                for c in range(CH):
                    dve.bn_stats(stats[:, c, :], xbuf[:, k % UNROLL, c, :]).then_inc(bn_done, 1)

            def guess(i):
                dve.wait_ge(var_done, at(i, 1, 1))
                dve.tensor_scalar(rstd[:, :].bitcast(I32), var_eps[:, :].bitcast(I32), -0.5, RSQRT_BITS,
                                  ALU.mult, ALU.add).then_inc(guess_done, 1)

            def norm(i, k, chunks):
                dve.wait_ge(rstd_done, at(i, 1, 1))
                dve.wait_ge(xT_ready, at(i, KD, 0))
                for c in chunks:
                    dve.tensor_scalar(xn[:, c, :], xbuf[:, k % UNROLL, c, :], mean[:, c:c + 1],
                                      rstd[:, c:c + 1], ALU.subtract, ALU.mult).then_inc(xn_done, 1)

            def xT_low(i, k):
                for half in range(KD):
                    dve.wait_ge(xTh_done, at(i, KD, half + 1))
                    dve.tensor_tensor(xT_l[:, k % 2, half, :], m_bank[half][:, :], xT_h[:, k % 2, half, :],
                                      ALU.subtract).then_inc(xTl_done, 1)

            def z_low(i, k):
                dve.wait_ge(zh_done, at(i, 1, 1))
                rows = slice(PR + 2 * R, P)
                dve.tensor_tensor(z_st[rows, k % 2, :], m_bank[0][rows, :], z_st[rows, k % 2, :],
                                  ALU.subtract).then_inc(zl_done, 1)

            def t_low(i):
                dve.wait_ge(th_done, at(i, 1, 1))
                dve.tensor_tensor(t_l[:, :], m_bank[1][:, :], t_h[:, :], ALU.subtract).then_inc(tl_done, 1)

            def scan(i, k):
                dve.wait_ge(uz_ready, at(i, 1, 1))
                dve.wait_ge(lam_done, at(i, 1, 1))
                before = 0.0
                if k % TPS:
                    before = s_seq[:, (k - 1) % 2, TOK - 1:TOK]
                dve.tensor_tensor_scan(s_seq[:, k % 2, :], lam[:, :], m_bank[0][0:PR, :], before,
                                       ALU.mult, ALU.add).then_inc(scan_done, 1)
                dve.wait_ge(scan_done, at(i, 1, 1))
                dve.wait_ge(t_ready, at(i, 1, 0))
                dve.tensor_copy(s_st[0:PR, :], s_seq[:, k % 2, :]).then_inc(sh_done, 1)
                dve.wait_ge(sh_done, at(i, 1, 1))
                dve.tensor_tensor(s_st[PR:P, :], s_seq[:, k % 2, :], s_st[0:PR, :],
                                  ALU.subtract).then_inc(sl_done, 1)

            def split_q(i, h):
                dve.wait_ge(q_done, at(i, H, h + 1))
                dve.wait_ge(q_used, at(i, H, h + 1 - QR))
                dve.tensor_copy(q_h[:, h % QR, :], q_buf[:, h % QR, :]).then_inc(qh_done, 1)
                dve.wait_ge(qh_done, at(i, H, h + 1))
                dve.tensor_tensor(q_l[:, h % QR, :], q_buf[:, h % QR, :], q_h[:, h % QR, :],
                                  ALU.subtract).then_inc(ql_done, 1)

            def add_residual(i, k):
                dve.wait_ge(stored[k % 2], at(i, 8, 16 - 8 * (k % 2) - 16))
                for j in range(2):
                    dve.wait_ge(oT_ready, at(i, 2, j + 1))
                    cs = slice(2 * j, 2 * j + 2)
                    dve.tensor_tensor(obuf[:, k % 2, cs, :],
                                      m_bank[1 + 2 * j][:, :].rearrange("p (c d) -> p c d", c=2),
                                      xbuf[:, k % UNROLL, cs, :], ALU.add).then_inc(added, 1)

            moments(0, 0)
            guess(0)
            norm(0, 0, range(CH))

            dve.wait_ge(w_loaded["fc"], 16)
            link(dve.tensor_reduce(s1[:, :], wfc_nat[:, :, :], AX.X, ALU.add, apply_absolute_value=True))
            link(dve.tensor_scalar(s1[:, :], s1[:, :], 1.0 / D, 1e-5, ALU.mult, ALU.max))
            dve.tensor_scalar(s1_half[:, :], s1[:, :], 0.5, None, ALU.mult)
            link(dve.tensor_scalar(s1_neg[:, :], s1[:, :], -0.5, None, ALU.mult))
            for h in range(H):
                ins = dve.tensor_scalar(t1_nat[:, h, :], wfc_nat[:, h, :], s1_neg[:, h:h + 1], None, ALU.is_lt)
            link(ins)
            for h in range(H):
                dve.scalar_tensor_tensor(out=t1_nat[:, h, :], in0=wfc_nat[:, h, :], scalar=s1_half[:, h:h + 1],
                                         in1=t1_nat[:, h, :], op0=ALU.is_gt, op1=ALU.subtract).then_inc(t1_ready, 1)
            dve.wait_ge(w_loaded["proj"], 16)
            link(dve.tensor_reduce(s2[:, :], wpj_nat[:, :, :], AX.X, ALU.add, apply_absolute_value=True))
            link(dve.tensor_scalar(s2[:, :], s2[:, :], 1.0 / HID, 1e-5, ALU.mult, ALU.max))
            dve.tensor_scalar(s2_half[:, :], s2[:, :], 0.5, None, ALU.mult)
            dve.reciprocal(s2_inv[:, :], s2[:, :])
            link(dve.tensor_scalar(s2_neg[:, :], s2[:, :], -0.5, None, ALU.mult))
            for g in range(KD):
                ins = dve.tensor_scalar(t2_nat[:, g, :], wpj_nat[:, g, :], s2_neg[:, g:g + 1], None, ALU.is_lt)
            link(ins)
            for g in range(KD):
                dve.scalar_tensor_tensor(out=t2_nat[:, g, :], in0=wpj_nat[:, g, :], scalar=s2_half[:, g:g + 1],
                                         in1=t2_nat[:, g, :], op0=ALU.is_gt, op1=ALU.subtract).then_inc(t2_ready, 1)

            dve.wait_ge(w_loaded["top"], 16)
            dve.wait_ge(w_loaded["u"], 16)
            dve.wait_ge(w_loaded["small"], 16 * 11)
            for kd in range(KD):
                ins = dve.tensor_tensor(wu_nat[:, kd, :], wu_nat[:, kd, :], wv_all[:, :], ALU.mult)
            link(ins)
            link(dve.tensor_reduce(wt_nat[:, :, :], wu_nat[:, :, :].rearrange("p k (n a) -> p (k n) a", a=AL),
                                   AX.X, ALU.add))
            dve.tensor_tensor(wt_nat[:, :, :], wt_nat[:, :, :], wtop_nat[:, :, :], ALU.add).then_inc(wt_ready, 1)
            dve.wait_ge(wt_ready, 1)
            for hi, of in ((wt_h, wt_nat), (wf_h, wf_nat), (wlam_h, wlam_nat), (cc_h, cc_nat)):
                ins = dve.tensor_copy(hi[:], of[:])
            link(ins)
            for lo, hi, of in ((wt_l, wt_h, wt_nat), (wf_l, wf_h, wf_nat), (wlam_l, wlam_h, wlam_nat),
                               (cc_l, cc_h, cc_nat)):
                ins = dve.tensor_tensor(lo[:], of[:], hi[:], ALU.subtract)
            link(ins)
            link(dve.reciprocal(s1_inv[:, :], s1[:, :]))
            link(dve.tensor_scalar(gate_s1[:, :], s1_inv[:, :], gate_all[:, 0:1], None, ALU.mult))

            xT_low(0, 0)
            outs = [0]

            def read_out():
                outs[0] += 1
                dve.wait_ge(prep_pe, outs[0])
                return bank[(outs[0] - 1) % 8]

            vb = read_out()
            for kd in range(KD):
                for n in range(4):
                    ins = dve.tensor_copy(uz_nat[:, kd, PR + n * R:PR + (n + 1) * R], vb[:, kd * R:(kd + 1) * R])
            ins.then_inc(prep_out, 1)
            b = read_out()
            dve.tensor_copy(wtT[:, :], b[:, 0:D]).then_inc(prep_out, 1)
            b = read_out()
            for g in range(KD):
                ins = dve.tensor_scalar(wfromT[:, g, :], b[:, g * P:(g + 1) * P], s2_inv[:, g:g + 1], None, ALU.mult)
            ins.then_inc(prep_out, 1)
            for n in range(2):
                b = read_out()
                dve.tensor_copy(uT[:, n * TOK:(n + 1) * TOK], b[0:R, :]).then_inc(prep_out, 1)
            b = read_out()
            link(dve.tensor_copy(uz_nat[:, :, 0:PR], b[:, 0:KD * PR].rearrange("p (k n) -> p k n", k=KD)))
            dve.tensor_copy(uz_h[:, :, :], uz_nat[:, :, :]).then_inc(prep_out, 1)
            dve.wait_ge(prep_out, outs[0])
            link(dve.tensor_tensor(uz_l[:, :, :], uz_nat[:, :, :], uz_h[:, :, :], ALU.subtract))
            b = read_out()
            link(dve.tensor_copy(wfrom_h[:, :], b[:, 0:D]))
            dve.tensor_tensor(wfrom_l[:, :], b[:, 0:D], wfrom_h[:, :], ALU.subtract).then_inc(prep_out, 1)
            b = read_out()
            for h in range(H):
                ins = dve.tensor_scalar(low_nat[:, h, :], b[:, h * R:(h + 1) * R], gate_s1[:, h:h + 1], None, ALU.mult)
            ins.then_inc(prep_out, 1)
            dve.wait_ge(prep_out, outs[0])
            link(dve.tensor_copy(low_hr[:, :, :], low_nat[:, :, :]))
            dve.wait_ge(zeros_ready, 1)
            for n in range(4):
                cols = slice(PR + n * R, PR + (n + 1) * R)
                if n % 2 == 0:
                    ins = dve.tensor_copy(low_rep[:, :, cols], low_hr[:, :, :])
                else:
                    ins = dve.tensor_tensor(low_rep[:, :, cols], low_nat[:, :, :], low_hr[:, :, :], ALU.subtract)
            ins.then_inc(low_ready, 1)
            for n in range(4):
                b = read_out()
                dve.tensor_copy(tern1[:, n // 2, (n % 2) * TOK:(n % 2 + 1) * TOK], b[:, :]).then_inc(prep_out, 1)
            for n in range(4):
                b = read_out()
                dve.tensor_copy(tern2[:, 2 * n:2 * n + 2, :], b[:, :].rearrange("p (h o) -> p h o", h=2)
                                ).then_inc(prep_out, 1)
            for n in range(2):
                b = read_out()
                if n == 0:
                    dve.tensor_copy(low_st[:, n * TOK:(n + 1) * TOK], b[:, :]).then_inc(prep_out, 1)
                else:
                    dve.tensor_copy(low_st[:, n * TOK:(n + 1) * TOK], b[:, :]).then_inc(weights_ready, 1)

            moments(1, 1)
            guess(1)
            norm(1, 1, range(CH))
            z_low(0, 0)
            scan(0, 0)

            def tile_steps(i, k):
                last = is_tile(i, NT - 1)
                two_more = not (isinstance(i, int) and i + 2 >= NT)
                for h in range(H):
                    if h == 0:
                        t_low(i)
                    if h == 1 and not last:
                        xT_low(i + 1, k + 1)
                    if h == 2 and two_more:
                        moments(i + 2, k + 2)
                    if h == 3 and two_more:
                        guess(i + 2)
                    if h == 4 and not last:
                        z_low(i + 1, k + 1)
                    if h == 5 and not is_tile(i, 0):
                        add_residual(i - 1, k - 1)
                    if h == 6 and not last:
                        scan(i + 1, k + 1)
                    if h == 7 and two_more:
                        norm(i + 2, k + 2, range(CH))
                    split_q(i, h)

            run_tiles(dve, tile_steps)
            add_residual(NT - 1, NT - 1)

        @block.tensor
        def _(pe):
            def split3(dst, parts, start, stop):
                n = 0
                for wh, wl, mh, ml in parts:
                    for w, m in ((wh, mh), (wh, ml), (wl, mh)):
                        ins = pe.matmul(dst, w, m, start=start and n == 0, stop=stop and n == 3 * len(parts) - 1)
                        n += 1
                return ins

            def turn_x(i):
                pe.wait_ge(xn_done, at(i, CH, CH))
                for half in range(KD):
                    if half == 0:
                        pe.wait_ge(scan_done, at(i, 1, 0))
                        pe.wait_ge(zl_done, at(i, 1, 0))
                    else:
                        pe.wait_ge(tl_done, at(i, 1, 0))
                    for c in range(CH):
                        ins = pe.transpose(m_bank[half][:, c * P:(c + 1) * P], xn[:, c, half * P:(half + 1) * P],
                                           ident[:, :])
                    ins.then_inc(xT_ready, 1)

            def xparts(wh, wl, k):
                return [(wh[:, kd, :], wl[:, kd, :], xT_h[:, k % 2, kd, :], xT_l[:, k % 2, kd, :])
                        for kd in range(KD)]

            def gate_product(i, k):
                pe.wait_ge(xTl_done, at(i, KD, KD))
                pe.wait_ge(lam_done, at(i, 1, 0))
                split3(m_bank[2][:, :], xparts(wf_h, wf_l, k), True, True).then_inc(f_ready, 1)

            def uz_product(i, k):
                pe.wait_ge(xTl_done, at(i, KD, KD))
                split3(m_bank[0][:, :], xparts(uz_h, uz_l, k), True, True).then_inc(uz_ready, 1)

            def decay_product(i):
                pe.wait_ge(fgl_done, at(i, 1, 1))
                split3(m_bank[2][0:PR, :], [(wlam_h[:, :], wlam_l[:, :], fg_h[:, :], fg_l[:, :])],
                       True, True).then_inc(laml_ready, 1)

            def t_product(i, k):
                pe.wait_ge(xTl_done, at(i, KD, KD))
                pe.wait_ge(added, at(i, 2, -3))
                split3(m_bank[1][:, :], xparts(wt_h, wt_l, k), True, False)

            def c_product(i):
                pe.wait_ge(sl_done, at(i, 1, 1))
                pe.matmul(m_bank[1][:, :], cc_h[:, :], s_st[:, :], start=False, stop=False)
                pe.matmul(m_bank[1][:, :], cc_l[:, :], s_st[:, :], start=False, stop=True).then_inc(t_ready, 1)

            def from_product(i):
                pe.wait_ge(tl_done, at(i, 1, 1))
                pe.wait_ge(y_done, at(i, KD, 0))
                for g in range(KD):
                    split3(y_bank[g][:, :], [(wfrom_h[:, g * P:(g + 1) * P], wfrom_l[:, g * P:(g + 1) * P],
                                              t_h[:, :], t_l[:, :])], True, False)

            def hidden(i, k, h):
                pe.wait_ge(r_done, at(i, H, h - 1))
                if h == 0:
                    pe.wait_ge(zl_done, at(i, 1, 1))
                dst = p_bank[h % 2][:, :]
                cols = slice(h * P, (h + 1) * P)
                for kd in range(KD):
                    for m in (xT_h, xT_l):
                        pe.matmul(dst, tern1[:, kd, cols], m[:, k % 2, kd, :], start=(kd == 0 and m is xT_h), stop=False)
                pe.matmul(dst, low_st[:, cols], z_st[:, k % 2, :], start=False, stop=True).then_inc(p_ready, 1)

            def project(i, h):
                pe.wait_ge(ql_done, at(i, H, h + 1))
                for g in range(KD):
                    for m in (q_h, q_l):
                        ins = pe.matmul(y_bank[g][:, :], tern2[:, h, g * P:(g + 1) * P], m[:, h % QR, :],
                                        start=False, stop=(h == H - 1 and m is q_l))
                ins.then_inc(q_used, 1)

            def turn_y(i):
                pe.wait_ge(y_done, at(i, KD, KD))
                for j in range(2):
                    if j == 0:
                        pe.wait_ge(tl_done, at(i, 1, 1))
                    else:
                        pe.wait_ge(added, at(i, 2, 0))
                    for n in range(2):
                        c = 2 * j + n
                        for g in range(KD):
                            ins = pe.transpose(m_bank[1 + 2 * j][:, n * D + g * P:n * D + (g + 1) * P],
                                               yT[:, g, c * P:(c + 1) * P], ident[:, :])
                    ins.then_inc(oT_ready, 1)

            pe.wait_ge(ident_ready, 2)
            turn_x(0)
            pe.wait_ge(xTl_done, KD)
            outs = [0]

            def prep_bank():
                outs[0] += 1
                if outs[0] > 8:
                    pe.wait_ge(prep_out, outs[0] - 8)
                return bank[(outs[0] - 1) % 8]

            pe.wait_ge(w_loaded["small"], 16 * 11)
            b = prep_bank()
            for kd in range(KD):
                ins = pe.transpose(b[:, kd * R:(kd + 1) * R], v_nat[:, kd * P:(kd + 1) * P], ident[0:R, 0:R])
            ins.then_inc(prep_pe, 1)
            pe.wait_ge(wt_ready, 1)
            b = prep_bank()
            for kd in range(KD):
                ins = pe.transpose(b[:, kd * P:(kd + 1) * P], wt_nat[:, kd, :], ident[:, :])
            ins.then_inc(prep_pe, 1)
            b = prep_bank()
            for g in range(KD):
                ins = pe.transpose(b[:, g * P:(g + 1) * P], wfrom_nat[:, g * P:(g + 1) * P], ident[:, :])
            ins.then_inc(prep_pe, 1)
            for n in range(2):
                b = prep_bank()
                for m in range(4):
                    ins = pe.transpose(b[0:R, m * P:(m + 1) * P], u_nat[:, 4 * n + m, :], ident[:, :])
                ins.then_inc(prep_pe, 1)
            b = prep_bank()
            pe.wait_ge(prep_out, 2)
            for kd in range(KD):
                ins = pe.matmul(b[:, kd * PR:(kd + 1) * PR], wtT[:, kd * P:(kd + 1) * P], b_nat[:, :],
                                start=True, stop=True)
            ins.then_inc(prep_pe, 1)
            b = prep_bank()
            pe.wait_ge(prep_out, 3)
            for g in range(KD):
                ins = pe.transpose(b[:, g * P:(g + 1) * P], wfromT[:, g, :], ident[:, :])
            ins.then_inc(prep_pe, 1)
            b = prep_bank()
            pe.wait_ge(prep_out, 5)
            for h in range(H):
                ins = pe.matmul(b[:, h * R:(h + 1) * R], uT[:, h * P:(h + 1) * P], fb_nat[:, :],
                                start=True, stop=True)
            ins.then_inc(prep_pe, 1)
            pe.wait_ge(t1_ready, H)
            for n in range(4):
                b = prep_bank()
                for m in range(4):
                    ins = pe.transpose(b[:, m * P:(m + 1) * P],
                                       t1_nat[:, 4 * (n % 2) + m, (n // 2) * P:(n // 2 + 1) * P], ident[:, :])
                ins.then_inc(prep_pe, 1)
            pe.wait_ge(t2_ready, KD)
            for n in range(4):
                b = prep_bank()
                for m in range(4):
                    h, g = 2 * n + m // 2, m % 2
                    ins = pe.transpose(b[:, m * P:(m + 1) * P], t2_nat[:, g, h * P:(h + 1) * P], ident[:, :])
                ins.then_inc(prep_pe, 1)
            pe.wait_ge(low_ready, 1)
            for n in range(2):
                b = prep_bank()
                for m in range(4):
                    ins = pe.transpose(b[:, m * P:(m + 1) * P], low_rep[:, 4 * n + m, :], ident[:, :])
                ins.then_inc(prep_pe, 1)

            pe.wait_ge(weights_ready, 1)
            pe.wait_ge(zeros_ready, 2)
            gate_product(0, 0)
            uz_product(0, 0)
            decay_product(0)
            t_product(0, 0)
            c_product(0)

            def tile_steps(i, k):
                first, last = is_tile(i, 0), is_tile(i, NT - 1)
                for h in range(H):
                    hidden(i, k, h)
                    if not last:
                        if h == 0:
                            turn_x(i + 1)
                        if h == 2:
                            gate_product(i + 1, k + 1)
                        if h == 3:
                            uz_product(i + 1, k + 1)
                        if h == 5:
                            decay_product(i + 1)
                        if h == 6:
                            t_product(i + 1, k + 1)
                        if h == 7:
                            c_product(i + 1)
                    if h == 4 and not first:
                        turn_y(i - 1)
                    if h == LAG:
                        from_product(i)
                    if h >= LAG:
                        project(i, h - LAG)
                    elif not first:
                        project(i - 1, h - LAG + H)

            run_tiles(pe, tile_steps)
            for h in range(H - LAG, H):
                project(NT - 1, h)
            turn_y(NT - 1)


_INS = ["x", "W_toP", "W_U", "W_F", "W_V", "W_lam", "B_mat", "C_mat", "W_fromP"]
_FFN = ["fast_b", "w_fc", "w_proj", "u", "v", "gate"]


def kernel(**inputs):
    import numpy as np
    import concourse.bacc as bacc
    from concourse.bass_utils import run_bass_kernel_spmd

    nc = bacc.Bacc("TRN2", target_bir_lowering=False, num_devices=1)
    arrays, args = {}, []
    for name in [f"L0_attn_{n}" for n in _INS] + [f"L0_ffn_{n}" for n in _FFN]:
        a = np.ascontiguousarray(inputs[name])
        if a.ndim == 0:
            a = a.reshape(1, 1)
        arrays[name] = a
        args.append(nc.dram_tensor(name, a.shape, mybir.dt.from_np(a.dtype), kind="ExternalInput").ap())
    shape = np.asarray(inputs["L0_attn_x"]).shape
    args.append(nc.dram_tensor("out", shape, F32, kind="ExternalOutput").ap())
    build(nc, *args)
    r = run_bass_kernel_spmd(nc, [arrays], core_ids=[0])
    return r.results[0]["out"]
```

```python
from contextlib import ExitStack

import concourse.bass as bass
from concourse import mybir

F32 = mybir.dt.float32
F32R = mybir.dt.float32r
I32 = mybir.dt.int32
ALU = mybir.AluOpType
ACT = mybir.ActivationFunctionType
AX = mybir.AxisListType

P = 128
TOK = 512
CH = TOK // P
UNROLL = 4
LAG = 2
QR = 4
EPS = 1e-5
NEWTON = 3
POOL_STEPS = 4 + 4 * NEWTON - 1
RSQRT_BITS = float(0x5F3759DF)


def at(tile, per, more):
    value = tile * per + more
    return max(value, 0) if isinstance(value, int) else value


def ring_dma(tile, slot, ring):
    return at(tile, 16 // ring, 16 - slot * 16 // ring)


def build(nc, x, W_toP, W_U, W_F, W_V, W_lam, B_mat, C_mat, W_fromP, fast_b, w_fc, w_proj, u, v, gate, out):
    NB, T, D = x.shape
    HID = w_fc.shape[0]
    PR = W_lam.shape[1]
    R = fast_b.shape[0]
    AL = W_V.shape[1]
    NT = NB * T // TOK
    TPS = T // TOK
    KD = D // P
    H = HID // P
    assert (KD, H, CH, TPS) == (2, 8, 4, 2) and PR == 64 and 4 * R == P - PR and NT % UNROLL == 0

    x_t = x.rearrange("b t d -> (b t) d").rearrange("(n c p) d -> n p c d", c=CH, p=P)
    out_t = out.rearrange("b t d -> (b t) d").rearrange("(n c p) d -> n p c d", c=CH, p=P)

    with ExitStack() as ctx:
        def sb(name, shape, dt=F32):
            return ctx.enter_context(nc.sbuf_tensor(name, shape, dt))

        def sem(name):
            return ctx.enter_context(nc.semaphore(name))

        wfc_nat = sb("wfc_nat", [P, H, D])
        wpj_nat = sb("wpj_nat", [P, KD, HID])
        wtop_nat = sb("wtop_nat", [P, KD, P])
        wu_nat = sb("wu_nat", [P, KD, P * AL])
        wv_all = sb("wv_all", [P, P * AL])
        wf_nat = sb("wf_nat", [P, KD, P])
        wlam_nat = sb("wlam_nat", [P, PR])
        b_nat = sb("b_nat", [P, PR])
        cc_nat = sb("cc_nat", [P, P])
        wfrom_nat = sb("wfrom_nat", [P, D])
        fb_nat = sb("fb_nat", [R, R])
        u_nat = sb("u_nat", [P, H, R])
        v_nat = sb("v_nat", [R, D])
        gate_all = sb("gate_all", [P, 1])
        ident = sb("ident", [P, P])
        sigmoid_ahead = sb("sigmoid_ahead", [P, CH])

        tern1 = sb("tern1", [P, KD, HID], F32R)
        tern2 = sb("tern2", [P, H, D], F32R)
        low_st = sb("low_st", [P, HID], F32R)
        wt_h = sb("wt_h", [P, KD, P], F32R)
        wt_l = sb("wt_l", [P, KD, P], F32R)
        wf_h = sb("wf_h", [P, KD, P], F32R)
        wf_l = sb("wf_l", [P, KD, P], F32R)
        uz_h = sb("uz_h", [P, KD, P], F32R)
        uz_l = sb("uz_l", [P, KD, P], F32R)
        wlam_hl = sb("wlam_hl", [P, P], F32R)
        cc_h = sb("cc_h", [P, P], F32R)
        cc_l = sb("cc_l", [P, P], F32R)
        wfrom_h = sb("wfrom_h", [P, D], F32R)
        wfrom_l = sb("wfrom_l", [P, D], F32R)
        s1 = sb("s1", [P, H])
        s2 = sb("s2", [P, KD])

        s1_half = sb("s1_half", [P, H])
        s1_neg = sb("s1_neg", [P, H])
        s2_half = sb("s2_half", [P, KD])
        s2_neg = sb("s2_neg", [P, KD])
        s2_inv = sb("s2_inv", [P, KD])
        s1_inv = sb("s1_inv", [P, H])
        gate_s1 = sb("gate_s1", [P, H])
        sign1 = sb("sign1", [P, H, D])
        sign2 = sb("sign2", [P, KD, HID])
        wt_nat = sb("wt_nat", [P, KD, P])
        wtT = sb("wtT", [P, D])
        uz_nat = sb("uz_nat", [P, KD, P])
        wfromT = sb("wfromT", [P, KD, P])
        uT = sb("uT", [R, HID])
        low_nat = sb("low_nat", [P, H, R])
        low_hr = sb("low_hr", [P, H, R], F32R)
        low_rep = sb("low_rep", [P, H, P])

        xbuf = sb("xbuf", [P, UNROLL, CH, D])
        stats = sb("stats", [P, CH, 6])
        mean = sb("mean", [P, CH])
        m_dif = sb("m_dif", [P, CH])
        var_eps = sb("var_eps", [P, CH])
        var_half = sb("var_half", [P, CH])
        c_half, c_quarter, c_minus_half, c_three_half, c_count, c_eps = (
            sb(f"c_{n}", [P, CH]) for n in ("half", "quarter", "minus_half", "three_half", "count", "eps"))
        rstd = sb("rstd", [P, CH])
        newton = sb("newton", [P, CH])
        xn = sb("xn", [P, CH, D])
        xT_h = sb("xT_h", [P, 2, KD, TOK], F32R)
        xT_l = sb("xT_l", [P, 2, KD, TOK], F32R)
        fg = sb("fg", [P, TOK])
        fg_h = sb("fg_h", [P, TOK], F32R)
        fg_l = sb("fg_l", [P, TOK], F32R)
        decay_lo = sb("decay_lo", [PR, TOK])
        decay_in = sb("decay_in", [PR, TOK])
        lam = sb("lam", [PR, TOK])
        s_seq = sb("s_seq", [PR, 2, TOK])
        s_st = sb("s_st", [P, TOK], F32R)
        z_st = sb("z_st", [P, 2, TOK], F32R)
        t_h = sb("t_h", [P, TOK], F32R)
        t_l = sb("t_l", [P, TOK], F32R)
        r_buf = sb("r_buf", [P, 2, TOK])
        q_buf = sb("q_buf", [P, QR, TOK])
        q_h = sb("q_h", [P, QR, TOK], F32R)
        q_l = sb("q_l", [P, QR, TOK], F32R)
        yT = sb("yT", [P, KD, TOK])
        obuf = sb("obuf", [P, 2, CH, D])

        abs_out = q_buf[:, 0:KD, :].rearrange("p a b -> p (a b)")

        bank = [ctx.enter_context(nc.psum_tensor(f"bank{n}", [P, TOK], F32)) for n in range(8)]
        p_bank = bank[0:2]
        y_bank = bank[2:4]
        m_bank = bank[4:8]

        w_loaded = {n: sem(f"w_loaded_{n}") for n in ("u", "fc", "v", "b", "low", "gate", "mat", "proj", "from")}
        x_loaded = [sem(f"x_loaded{n}") for n in range(UNROLL)]
        stored = [sem(f"stored{n}") for n in range(2)]
        ident_ready = sem("ident_ready")
        zeros_ready = sem("zeros_ready")
        abs1_done = sem("abs1_done")
        abs2_done = sem("abs2_done")
        s1_ready = sem("s1_ready")
        s2_ready = sem("s2_ready")
        split_hi = sem("split_hi")
        split_lo = sem("split_lo")
        uz_h_done = sem("uz_h_done")
        wfrom_h_done = sem("wfrom_h_done")
        low_h_done = sem("low_h_done")
        prep_pe = sem("prep_pe")
        prep_act = sem("prep_act")
        prep_vec = sem("prep_vec")
        prep_dve = sem("prep_dve")
        below1_done = sem("below1_done")
        below2_done = sem("below2_done")
        sign1_ready = sem("sign1_ready")
        sign2_ready = sem("sign2_ready")
        wt_ready = sem("wt_ready")
        low_ready = sem("low_ready")
        wt_split = sem("wt_split")
        uz_split = sem("uz_split")
        bn_done = sem("bn_done")
        var_done = sem("var_done")
        guess_done = sem("guess_done")
        pool_steps = sem("pool_steps")
        rstd_done = sem("rstd_done")
        xn_done = sem("xn_done")
        xT_ready = sem("xT_ready")
        xTh_done = sem("xTh_done")
        xTl_done = sem("xTl_done")
        f_ready = sem("f_ready")
        fgh_done = sem("fgh_done")
        fgl_done = sem("fgl_done")
        uz_ready = sem("uz_ready")
        zh_done = sem("zh_done")
        zl_done = sem("zl_done")
        decay_ready = sem("decay_ready")
        decay_lo_done = sem("decay_lo_done")
        decay_in_done = sem("decay_in_done")
        lam_done = sem("lam_done")
        scan_done = sem("scan_done")
        sh_done = sem("sh_done")
        sl_done = sem("sl_done")
        t_ready = sem("t_ready")
        th_done = sem("th_done")
        tl_done = sem("tl_done")
        p_ready = sem("p_ready")
        r_done = sem("r_done")
        q_done = sem("q_done")
        qh_done = sem("qh_done")
        ql_done = sem("ql_done")
        q_used = sem("q_used")
        y0_done = sem("y0_done")
        y1_done = sem("y1_done")
        oT_ready = sem("oT_ready")
        added = sem("added")

        prep_banks = [bank[n] for n in (0, 1, 2, 3, 7, 0, 0, 1, 2, 3, 7, 1, 2, 3, 2, 3, 2, 3)]
        readers = ["act",
                   "vec",
                   "act", "act",
                   "vec",
                   "vec",
                   "act", "act", "act", "act",
                   "act", "act",
                   "act",
                   "act", "act", "act", "act",
                   "vec"]
        V_STEP, WT_STEP, U_STEP, WTB_STEP, LOW_STEP, T1_STEP, LST_STEP, WFT_STEP, T2_STEP, WF_STEP = (
            0, 1, 2, 4, 5, 6, 10, 12, 13, 17)

        def prep_bank(step):
            return prep_banks[step]

        def wait_read(eng, step):
            who = readers[step]
            eng.wait_ge(prep_act if who == "act" else prep_vec, readers[:step + 1].count(who))

        block = ctx.enter_context(nc.Block())

        def run_tiles(eng, tile_steps):
            for i in range(UNROLL):
                tile_steps(i, i)
            with eng.Fori(1, NT // UNROLL - 1) as turn:
                for k in range(UNROLL):
                    tile_steps(turn * UNROLL + k, k)
            for k in range(UNROLL):
                tile_steps(NT - UNROLL + k, k)

        def is_tile(i, n):
            return isinstance(i, int) and i == n

        @block.sync
        def _(sp):
            def load(dst, src, name):
                sp.dma_start(dst, src).then_inc(w_loaded[name], 16)

            sp.dma_start(xbuf[:, 0, :, :], x_t[0]).then_inc(x_loaded[0], 16)
            load(wu_nat[:, :, :], W_U.rearrange("(k p) n a -> p k (n a)", p=P), "u")
            load(wfc_nat[:, :, :], w_fc.rearrange("(h p) d -> p h d", p=P), "fc")
            load(fb_nat[:, :], fast_b, "low")
            load(wf_nat[:, :, :], W_F.rearrange("(k p) n -> p k n", p=P), "mat")
            load(cc_nat[0:PR, :], C_mat, "mat")
            load(cc_nat[PR:P, :], C_mat, "mat")
            load(wpj_nat[:, :, :], w_proj.rearrange("(g p) h -> p g h", p=P), "proj")
            load(wfrom_nat[:, :], W_fromP, "from")
            for n in range(1, UNROLL):
                sp.dma_start(xbuf[:, n, :, :], x_t[n]).then_inc(x_loaded[n], 16)

            def tile_steps(i, k):
                if is_tile(i, 0):
                    return
                sp.wait_ge(added, at(i, 2, 0))
                sp.dma_start(out_t[bass.ds(i - 1, 1)].rearrange("n p c d -> p (n c) d"),
                             obuf[:, (k - 1) % 2, :, :]).then_inc(stored[(k - 1) % 2], 16)
                if isinstance(i, int) and i + 3 >= NT:
                    return
                sp.dma_start(xbuf[:, (k + 3) % UNROLL, :, :],
                             x_t[bass.ds(i + 3, 1)].rearrange("n p c d -> p (n c) d")
                             ).then_inc(x_loaded[(k + 3) % UNROLL], 16)

            run_tiles(sp, tile_steps)
            for j in range(2):
                sp.wait_ge(added, 2 * NT - 1 + j)
                cs = slice(2 * j, 2 * j + 2)
                sp.dma_start(out_t[NT - 1][:, cs, :], obuf[:, (NT - 1) % 2, cs, :]
                             ).then_inc(stored[(NT - 1) % 2], 16)
            for n in range(2):
                sp.wait_ge(stored[n], 16 * (NT // 2 + (n == (NT - 1) % 2)))

        @block.gpsimd
        def _(pool):
            pool.memset(ident[:, :], 0.0).then_inc(ident_ready, 1)
            pool.wait_ge(ident_ready, 1)
            pool.affine_select(out=ident[:, :], in_=ident[:, :], compare_op=ALU.not_equal, fill=1.0,
                               base=0, pattern=[[-1, P]], channel_multiplier=1).then_inc(ident_ready, 1)
            for tile, value in ((c_half, 0.5), (c_quarter, 0.25), (c_minus_half, -0.5), (c_three_half, 1.5),
                                (c_count, 1.0 / D), (c_eps, EPS)):
                ins = pool.memset(tile[:, :], value)
            ins.then_inc(ident_ready, 1)
            pool.memset(low_rep[:, :, 0:PR], 0.0).then_inc(zeros_ready, 1)
            pool.memset(z_st[0:PR, :, :].bitcast(F32), 0.0).then_inc(zeros_ready, 1)

            def moments_of(i):
                steps = [0]

                def link(ins):
                    steps[0] += 1
                    ins.then_inc(pool_steps, 1)
                    pool.wait_ge(pool_steps, at(i, POOL_STEPS, steps[0]))

                tt = pool.tensor_tensor
                pool.wait_ge(bn_done, at(i, CH, CH))
                pool.wait_ge(xn_done, at(i, CH, 0))
                tt(mean[:, :], stats[:, :, 1], stats[:, :, 4], ALU.add)
                tt(m_dif[:, :], stats[:, :, 1], stats[:, :, 4], ALU.subtract)
                link(tt(var_eps[:, :], stats[:, :, 2], stats[:, :, 5], ALU.add))
                tt(mean[:, :], mean[:, :], c_half[:, :], ALU.mult)
                tt(m_dif[:, :], m_dif[:, :], m_dif[:, :], ALU.mult)
                link(tt(var_eps[:, :], var_eps[:, :], c_count[:, :], ALU.mult))
                tt(m_dif[:, :], m_dif[:, :], c_quarter[:, :], ALU.mult)
                link(tt(var_eps[:, :], var_eps[:, :], c_eps[:, :], ALU.add))
                link(tt(var_eps[:, :], var_eps[:, :], m_dif[:, :], ALU.add))
                tt(var_half[:, :], var_eps[:, :], c_minus_half[:, :], ALU.mult).then_inc(var_done, 1)
                pool.wait_ge(guess_done, at(i, 1, 1))
                for n in range(NEWTON):
                    link(tt(newton[:, :], rstd[:, :], rstd[:, :], ALU.mult))
                    link(tt(newton[:, :], newton[:, :], var_half[:, :], ALU.mult))
                    link(tt(newton[:, :], newton[:, :], c_three_half[:, :], ALU.add))
                    ins = tt(rstd[:, :], rstd[:, :], newton[:, :], ALU.mult)
                    if n < NEWTON - 1:
                        link(ins)
                    else:
                        ins.then_inc(rstd_done, 1)
                assert steps[0] == POOL_STEPS

            def fg_low(i):
                pool.wait_ge(fgh_done, at(i, 1, 1))
                pool.wait_ge(decay_ready, at(i, 1, 0))
                pool.tensor_tensor(fg_l[:, :], fg[:, :], fg_h[:, :], ALU.subtract).then_inc(fgl_done, 1)

            pool.wait_ge(ident_ready, 3)
            moments_of(0)
            pool.wait_ge(split_hi, 3)
            for lo, hi, of in ((wf_l[:, :, :], wf_h[:, :, :], wf_nat[:, :, :]),
                               (wlam_hl[:, PR:P], wlam_hl[:, 0:PR], wlam_nat[:, :]),
                               (cc_l[:, :], cc_h[:, :], cc_nat[:, :])):
                pool.tensor_tensor(lo, of, hi, ALU.subtract).then_inc(split_lo, 1)
            fg_low(0)
            moments_of(1)

            def tile_steps(i, k):
                if not is_tile(i, NT - 1):
                    fg_low(i + 1)
                if not (isinstance(i, int) and i + 2 >= NT):
                    moments_of(i + 2)

            run_tiles(pool, tile_steps)

        @block.scalar
        def _(act):
            def load(dst, src, name):
                act.dma_start(dst, src).then_inc(w_loaded[name], 16)

            load(wv_all[:, :], W_V.rearrange("n a -> (n a)").rearrange("(o m) -> o m", o=1)
                 .broadcast_to([P, P * AL]), "u")
            load(wtop_nat[:, :, :], W_toP.rearrange("(k p) n -> p k n", p=P), "u")
            load(v_nat[:, :], v, "v")
            load(b_nat[:, :], B_mat, "b")
            load(u_nat[:, :, :], u.rearrange("(h p) r -> p h r", p=P), "low")
            load(gate_all[:, :], gate.broadcast_to([P, 1]), "gate")
            load(wlam_nat[:, :], W_lam, "mat")

            def t_high(i):
                act.wait_ge(t_ready, at(i, 1, 1))
                act.wait_ge(q_used, at(i, H, 1 - H))
                act.activation(t_h[:, :], m_bank[3][:, :], ACT.Copy).then_inc(th_done, 1)

            def xT_high(i, k):
                for half in range(KD):
                    act.wait_ge(xT_ready, at(i, KD, half + 1))
                    act.wait_ge(p_ready, at(i, H, -H))
                    act.activation(xT_h[:, k % 2, half, :], m_bank[half][:, :], ACT.Copy).then_inc(xTh_done, 1)

            def gates(i):
                act.wait_ge(f_ready, at(i, 1, 1))
                act.wait_ge(fgl_done, at(i, 1, 0))
                act.activation(fg[:, :], m_bank[2][:, :], ACT.Sigmoid)
                act.wait_ge(decay_ready, at(i, 1, 0))
                act.activation(fg_h[:, :], m_bank[2][:, :], ACT.Sigmoid).then_inc(fgh_done, 1)

            def z_high(i, k):
                act.wait_ge(uz_ready, at(i, 1, 1))
                act.wait_ge(p_ready, at(i, H, -H))
                act.activation(z_st[PR:P, k % 2, :], m_bank[0][PR:P, :], ACT.Copy).then_inc(zh_done, 1)

            def decay_low(i):
                act.wait_ge(decay_ready, at(i, 1, 1))
                act.wait_ge(decay_in_done, at(i, 1, 0))
                act.activation(decay_lo[:, :], m_bank[2][PR:P, :], ACT.Copy).then_inc(decay_lo_done, 1)

            def decay(i):
                act.wait_ge(decay_in_done, at(i, 1, 1))
                act.wait_ge(scan_done, at(i, 1, 0))
                act.activation(lam[:, :], decay_in[:, :], ACT.Sigmoid).then_inc(lam_done, 1)

            def relu(i, h):
                act.wait_ge(p_ready, at(i, H, h + 1))
                act.wait_ge(q_done, at(i, H, h - 1))
                act.activation(r_buf[:, h % 2, :], p_bank[h % 2][:, :], ACT.Relu,
                               scale=s1[:, h:h + 1]).then_inc(r_done, 1)

            def square(i, h):
                act.wait_ge(r_done, at(i, H, h + 1))
                act.wait_ge(ql_done, at(i, H, h + 1 - QR))
                act.activation(q_buf[:, h % QR, :], r_buf[:, h % 2, :], ACT.Square).then_inc(q_done, 1)

            def y_scaled(i):
                act.wait_ge(q_used, at(i, H, H))
                act.wait_ge(oT_ready, at(i, 2, 0))
                act.activation(yT[:, 0, :], y_bank[0][:, :], ACT.Copy, scale=s2[:, 0:1]).then_inc(y0_done, 1)

            act.wait_ge(ident_ready, 3)
            act.activation(sigmoid_ahead[:, :], c_half[:, :], ACT.Sigmoid)
            act.wait_ge(w_loaded["fc"], 16)
            for h in range(H):
                if h:
                    act.wait_ge(abs1_done, h)
                act.activation(abs_out[:, 0:D], wfc_nat[:, h, :], ACT.Abs, accum_out=s1[:, h:h + 1]).then_inc(abs1_done, 1)
            act.wait_ge(w_loaded["mat"], 16 * 4)
            for hi, of in ((wf_h[:, :, :], wf_nat[:, :, :]), (wlam_hl[:, 0:PR], wlam_nat[:, :]),
                           (cc_h[:, :], cc_nat[:, :])):
                act.activation(hi, of, ACT.Copy).then_inc(split_hi, 1)

            def written(step):
                act.wait_ge(prep_pe, step + 1)
                return prep_bank(step)

            b = written(V_STEP)
            act.activation(uz_nat[:, :, PR:P], b[:, 0:KD * 4 * R].rearrange("p (k n) -> p k n", k=KD),
                           ACT.Copy).then_inc(prep_act, 1)
            xT_high(0, 0)
            for n in range(2):
                b = written(U_STEP + n)
                act.activation(uT[:, n * TOK:(n + 1) * TOK], b[0:R, :], ACT.Copy).then_inc(prep_act, 1)
            wait_read(act, WTB_STEP)
            wait_read(act, V_STEP)
            act.activation(uz_h[:, :, :], uz_nat[:, :, :], ACT.Copy).then_inc(uz_h_done, 1)
            act.wait_ge(w_loaded["proj"], 16)
            act.wait_ge(abs1_done, H)
            for g in range(KD):
                if g:
                    act.wait_ge(abs2_done, g)
                act.activation(abs_out, wpj_nat[:, g, :], ACT.Abs, accum_out=s2[:, g:g + 1]).then_inc(abs2_done, 1)
            gates(0)
            wait_read(act, LOW_STEP)
            act.activation(low_hr[:, :, :], low_nat[:, :, :], ACT.Copy).then_inc(low_h_done, 1)
            z_high(0, 0)
            for n in range(4):
                b = written(T1_STEP + n)
                act.activation(tern1[:, n // 2, (n % 2) * TOK:(n % 2 + 1) * TOK], b[:, :], ACT.Copy).then_inc(prep_act, 1)
            for n in range(2):
                b = written(LST_STEP + n)
                act.activation(low_st[:, n * TOK:(n + 1) * TOK], b[:, :], ACT.Copy).then_inc(prep_act, 1)
            decay_low(0)
            decay(0)

            def second_layer_out():
                b = written(WFT_STEP)
                act.wait_ge(s2_ready, 1)
                for g in range(KD):
                    ins = act.activation(wfromT[:, g, :], b[:, g * P:(g + 1) * P], ACT.Copy, scale=s2_inv[:, g:g + 1])
                ins.then_inc(prep_act, 1)
                for n in range(4):
                    b = written(T2_STEP + n)
                    act.activation(tern2[:, 2 * n:2 * n + 2, :], b[:, :].rearrange("p (h o) -> p h o", h=2),
                                   ACT.Copy).then_inc(prep_act, 1)
                b = written(WF_STEP)
                act.activation(wfrom_h[:, :], b[:, 0:D], ACT.Copy).then_inc(wfrom_h_done, 1)

            def tile_steps(i, k):
                last = is_tile(i, NT - 1)
                for h in range(H):
                    if h == 0 and not is_tile(i, 0):
                        t_high(i)
                    if h == 2 and not is_tile(i, 0):
                        y_scaled(i - 1)
                    relu(i, h)
                    if h == 5 and not last:
                        decay(i + 1)
                    square(i, h)
                    if is_tile(i, 0) and h == 0:
                        second_layer_out()
                        t_high(0)
                    if last:
                        continue
                    if h == 0:
                        xT_high(i + 1, k + 1)
                    if h == 2:
                        gates(i + 1)
                    if h == 3:
                        z_high(i + 1, k + 1)
                    if h == 4:
                        decay_low(i + 1)

            run_tiles(act, tile_steps)
            y_scaled(NT - 1)

        @block.vector
        def _(dve):
            links = [0]

            def link(ins):
                links[0] += 1
                ins.then_inc(prep_dve, 1)
                dve.wait_ge(prep_dve, links[0])

            def moments(i, k):
                dve.wait_ge(x_loaded[k % UNROLL], ring_dma(i, k % UNROLL, UNROLL))
                dve.wait_ge(var_done, at(i, 1, 0))
                for c in range(CH):
                    dve.bn_stats(stats[:, c, :], xbuf[:, k % UNROLL, c, :]).then_inc(bn_done, 1)

            def guess(i):
                dve.wait_ge(var_done, at(i, 1, 1))
                dve.tensor_scalar(rstd[:, :].bitcast(I32), var_eps[:, :].bitcast(I32), -0.5, RSQRT_BITS,
                                  ALU.mult, ALU.add).then_inc(guess_done, 1)

            def norm(i, k, chunks):
                dve.wait_ge(rstd_done, at(i, 1, 1))
                dve.wait_ge(xT_ready, at(i, KD, 0))
                for c in chunks:
                    dve.tensor_scalar(xn[:, c, :], xbuf[:, k % UNROLL, c, :], mean[:, c:c + 1],
                                      rstd[:, c:c + 1], ALU.subtract, ALU.mult).then_inc(xn_done, 1)

            def xT_low(i, k):
                for half in range(KD):
                    dve.wait_ge(xTh_done, at(i, KD, half + 1))
                    dve.tensor_tensor(xT_l[:, k % 2, half, :], m_bank[half][:, :], xT_h[:, k % 2, half, :],
                                      ALU.subtract).then_inc(xTl_done, 1)

            def z_low(i, k):
                dve.wait_ge(zh_done, at(i, 1, 1))
                rows = slice(PR + 2 * R, P)
                dve.tensor_tensor(z_st[rows, k % 2, :], m_bank[0][rows, :], z_st[rows, k % 2, :],
                                  ALU.subtract).then_inc(zl_done, 1)

            def t_low(i):
                dve.wait_ge(th_done, at(i, 1, 1))
                dve.tensor_tensor(t_l[:, :], m_bank[3][:, :], t_h[:, :], ALU.subtract).then_inc(tl_done, 1)

            def decay_sum(i):
                dve.wait_ge(decay_lo_done, at(i, 1, 1))
                dve.wait_ge(lam_done, at(i, 1, 0))
                dve.tensor_tensor(decay_in[:, :], m_bank[2][0:PR, :], decay_lo[:, :], ALU.add
                                  ).then_inc(decay_in_done, 1)

            def scan(i, k):
                dve.wait_ge(uz_ready, at(i, 1, 1))
                dve.wait_ge(lam_done, at(i, 1, 1))
                before = 0.0
                if k % TPS:
                    before = s_seq[:, (k - 1) % 2, TOK - 1:TOK]
                dve.tensor_tensor_scan(s_seq[:, k % 2, :], lam[:, :], m_bank[0][0:PR, :], before,
                                       ALU.mult, ALU.add).then_inc(scan_done, 1)
                dve.wait_ge(scan_done, at(i, 1, 1))
                dve.wait_ge(t_ready, at(i, 1, 0))
                dve.tensor_copy(s_st[0:PR, :], s_seq[:, k % 2, :]).then_inc(sh_done, 1)
                dve.wait_ge(sh_done, at(i, 1, 1))
                dve.tensor_tensor(s_st[PR:P, :], s_seq[:, k % 2, :], s_st[0:PR, :],
                                  ALU.subtract).then_inc(sl_done, 1)

            def split_q(i, h):
                dve.wait_ge(q_done, at(i, H, h + 1))
                dve.wait_ge(q_used, at(i, H, h + 1 - QR))
                dve.tensor_copy(q_h[:, h % QR, :], q_buf[:, h % QR, :]).then_inc(qh_done, 1)
                dve.wait_ge(qh_done, at(i, H, h + 1))
                dve.tensor_tensor(q_l[:, h % QR, :], q_buf[:, h % QR, :], q_h[:, h % QR, :],
                                  ALU.subtract).then_inc(ql_done, 1)

            def add_residual(i, k):
                dve.wait_ge(stored[k % 2], at(i, 8, 16 - 8 * (k % 2) - 16))
                for j in range(2):
                    dve.wait_ge(oT_ready, at(i, 2, j + 1))
                    cs = slice(2 * j, 2 * j + 2)
                    dve.tensor_tensor(obuf[:, k % 2, cs, :],
                                      m_bank[1 + 2 * j][:, :].rearrange("p (c d) -> p c d", c=2),
                                      xbuf[:, k % UNROLL, cs, :], ALU.add).then_inc(added, 1)

            def y_scaled(i):
                dve.wait_ge(q_used, at(i, H, H))
                dve.wait_ge(oT_ready, at(i, 2, 0))
                dve.tensor_scalar(yT[:, 1, :], y_bank[1][:, :], s2[:, 1:2], None, ALU.mult).then_inc(y1_done, 1)

            moments(0, 0)
            dve.wait_ge(w_loaded["u"], 16 * 3)
            for kd in range(KD):
                ins = dve.tensor_tensor(wu_nat[:, kd, :], wu_nat[:, kd, :], wv_all[:, :], ALU.mult)
            link(ins)
            guess(0)
            link(dve.tensor_reduce(wt_nat[:, :, :], wu_nat[:, :, :].rearrange("p k (n a) -> p (k n) a", a=AL),
                                   AX.X, ALU.add))
            dve.tensor_tensor(wt_nat[:, :, :], wt_nat[:, :, :], wtop_nat[:, :, :], ALU.add).then_inc(wt_ready, 1)
            dve.wait_ge(wt_ready, 1)
            link(dve.tensor_copy(wt_h[:, :, :], wt_nat[:, :, :]))
            dve.tensor_tensor(wt_l[:, :, :], wt_nat[:, :, :], wt_h[:, :, :], ALU.subtract).then_inc(wt_split, 1)

            def scales(s, half, neg, inv, count, summed, ready):
                dve.wait_ge(*summed)
                link(dve.tensor_scalar(s[:, :], s[:, :], 1.0 / count, 1e-5, ALU.mult, ALU.max))
                dve.tensor_scalar(half[:, :], s[:, :], 0.5, None, ALU.mult)
                dve.reciprocal(inv[:, :], s[:, :])
                dve.tensor_scalar(neg[:, :], s[:, :], -0.5, None, ALU.mult).then_inc(ready, 1)
                dve.wait_ge(ready, 1)

            def written(step):
                dve.wait_ge(prep_pe, step + 1)
                return prep_bank(step)

            def below(sign, w, neg, rows, below_done):
                for n in rows:
                    dve.tensor_scalar(sign[:, n, :], w[:, n, :], neg[:, n:n + 1], None, ALU.is_lt
                                      ).then_inc(below_done, 1)

            def signs(sign, w, half, rows, below_done, ready):
                for n in rows:
                    dve.wait_ge(below_done, n + 1)
                    dve.scalar_tensor_tensor(sign[:, n, :], w[:, n, :], half[:, n:n + 1], sign[:, n, :],
                                             ALU.is_gt, ALU.subtract).then_inc(ready, 1)

            b = written(WT_STEP)
            dve.tensor_copy(wtT[:, :], b[:, 0:D]).then_inc(prep_vec, 1)
            norm(0, 0, range(CH))
            scales(s1, s1_half, s1_neg, s1_inv, D, (abs1_done, H), s1_ready)
            dve.wait_ge(w_loaded["gate"], 16)
            link(dve.tensor_scalar(gate_s1[:, :], s1_inv[:, :], gate_all[:, 0:1], None, ALU.mult))
            below(sign1, wfc_nat, s1_neg, range(H // 2), below1_done)
            xT_low(0, 0)
            b = written(WTB_STEP)
            dve.tensor_copy(uz_nat[:, :, 0:PR], b[:, 0:KD * PR].rearrange("p (k n) -> p k n", k=KD)
                            ).then_inc(prep_vec, 1)
            below(sign1, wfc_nat, s1_neg, range(H // 2, H), below1_done)
            dve.wait_ge(uz_h_done, 1)
            dve.tensor_tensor(uz_l[:, :, :], uz_nat[:, :, :], uz_h[:, :, :], ALU.subtract).then_inc(uz_split, 1)
            signs(sign1, wfc_nat, s1_half, range(H // 2), below1_done, sign1_ready)
            b = written(LOW_STEP)
            dve.tensor_tensor(low_nat[:, :, :], b[:, 0:H * R].rearrange("p (h r) -> p h r", h=H),
                              gate_s1[:, :].rearrange("p (h o) -> p h o", o=1).broadcast_to([P, H, R]),
                              ALU.mult).then_inc(prep_vec, 1)
            signs(sign1, wfc_nat, s1_half, range(H // 2, H), below1_done, sign1_ready)
            dve.wait_ge(low_h_done, 1)
            dve.wait_ge(zeros_ready, 1)
            for n in range(4):
                cols = slice(PR + n * R, PR + (n + 1) * R)
                if n % 2 == 0:
                    ins = dve.tensor_copy(low_rep[:, :, cols], low_hr[:, :, :])
                else:
                    ins = dve.tensor_tensor(low_rep[:, :, cols], low_nat[:, :, :], low_hr[:, :, :], ALU.subtract)
            ins.then_inc(low_ready, 1)
            z_low(0, 0)
            moments(1, 1)
            scales(s2, s2_half, s2_neg, s2_inv, HID, (abs2_done, KD), s2_ready)
            below(sign2, wpj_nat, s2_neg, range(KD), below2_done)
            decay_sum(0)
            guess(1)
            signs(sign2, wpj_nat, s2_half, range(KD), below2_done, sign2_ready)
            scan(0, 0)

            def tile_steps(i, k):
                last = is_tile(i, NT - 1)
                two_more = not (isinstance(i, int) and i + 2 >= NT)
                for h in range(H):
                    if h == 0 and is_tile(i, 0):
                        split_q(0, 0)
                        norm(1, 1, range(CH))
                        t_low(0)
                        continue
                    if h == 0:
                        t_low(i)
                    if h == 1 and is_tile(i, 0):
                        dve.wait_ge(wfrom_h_done, 1)
                        dve.tensor_tensor(wfrom_l[:, :], prep_bank(WF_STEP)[:, 0:D], wfrom_h[:, :],
                                          ALU.subtract).then_inc(prep_vec, 1)
                    if h == 1 and not last:
                        xT_low(i + 1, k + 1)
                    if h == 2 and not is_tile(i, 0):
                        y_scaled(i - 1)
                    if h == 2 and two_more:
                        moments(i + 2, k + 2)
                    if h == 4 and two_more:
                        guess(i + 2)
                    if h == 4 and not last:
                        z_low(i + 1, k + 1)
                    if h == 5 and not last:
                        decay_sum(i + 1)
                    if h == 5 and not is_tile(i, 0):
                        add_residual(i - 1, k - 1)
                    if h == 6 and not last:
                        scan(i + 1, k + 1)
                    if h == 7 and two_more:
                        norm(i + 2, k + 2, range(CH))
                    split_q(i, h)

            run_tiles(dve, tile_steps)
            y_scaled(NT - 1)
            add_residual(NT - 1, NT - 1)

        @block.tensor
        def _(pe):
            def split3(dst, parts, start, stop):
                n = 0
                for wh, wl, mh, ml in parts:
                    for w, m in ((wh, mh), (wh, ml), (wl, mh)):
                        ins = pe.matmul(dst, w, m, start=start and n == 0, stop=stop and n == 3 * len(parts) - 1)
                        n += 1
                return ins

            def turn_x(i):
                pe.wait_ge(xn_done, at(i, CH, CH))
                for half in range(KD):
                    if half == 0:
                        pe.wait_ge(scan_done, at(i, 1, 0))
                        pe.wait_ge(zl_done, at(i, 1, 0))
                    else:
                        pe.wait_ge(added, at(i, 2, -5))
                    for c in range(CH):
                        ins = pe.transpose(m_bank[half][:, c * P:(c + 1) * P], xn[:, c, half * P:(half + 1) * P],
                                           ident[:, :])
                    ins.then_inc(xT_ready, 1)

            def xparts(wh, wl, k):
                return [(wh[:, kd, :], wl[:, kd, :], xT_h[:, k % 2, kd, :], xT_l[:, k % 2, kd, :])
                        for kd in range(KD)]

            def gate_product(i, k):
                pe.wait_ge(xTl_done, at(i, KD, KD))
                pe.wait_ge(decay_in_done, at(i, 1, 0))
                split3(m_bank[2][:, :], xparts(wf_h, wf_l, k), True, True).then_inc(f_ready, 1)

            def uz_product(i, k):
                pe.wait_ge(xTl_done, at(i, KD, KD))
                split3(m_bank[0][:, :], xparts(uz_h, uz_l, k), True, True).then_inc(uz_ready, 1)

            def decay_product(i):
                pe.wait_ge(fgl_done, at(i, 1, 1))
                pe.matmul(m_bank[2][:, :], wlam_hl[:, :], fg_h[:, :], start=True, stop=False)
                pe.matmul(m_bank[2][:, :], wlam_hl[:, :], fg_l[:, :], start=False, stop=True).then_inc(decay_ready, 1)

            def t_product(i, k):
                pe.wait_ge(xTl_done, at(i, KD, KD))
                pe.wait_ge(added, at(i, 2, -2))
                split3(m_bank[3][:, :], xparts(wt_h, wt_l, k), True, False)

            def c_product(i):
                pe.wait_ge(sl_done, at(i, 1, 1))
                pe.matmul(m_bank[3][:, :], cc_h[:, :], s_st[:, :], start=False, stop=False)
                pe.matmul(m_bank[3][:, :], cc_l[:, :], s_st[:, :], start=False, stop=True).then_inc(t_ready, 1)

            def from_product(i):
                pe.wait_ge(tl_done, at(i, 1, 1))
                for g in range(KD):
                    pe.wait_ge((y0_done, y1_done)[g], at(i, 1, 0))
                    split3(y_bank[g][:, :], [(wfrom_h[:, g * P:(g + 1) * P], wfrom_l[:, g * P:(g + 1) * P],
                                              t_h[:, :], t_l[:, :])], True, False)

            def hidden(i, k, h):
                pe.wait_ge(r_done, at(i, H, h - 1))
                if h == 0:
                    pe.wait_ge(zl_done, at(i, 1, 1))
                dst = p_bank[h % 2][:, :]
                cols = slice(h * P, (h + 1) * P)
                for kd in range(KD):
                    for m in (xT_h, xT_l):
                        pe.matmul(dst, tern1[:, kd, cols], m[:, k % 2, kd, :], start=(kd == 0 and m is xT_h), stop=False)
                pe.matmul(dst, low_st[:, cols], z_st[:, k % 2, :], start=False, stop=True).then_inc(p_ready, 1)

            def project(i, h):
                pe.wait_ge(ql_done, at(i, H, h + 1))
                for g in range(KD):
                    for m in (q_h, q_l):
                        ins = pe.matmul(y_bank[g][:, :], tern2[:, h, g * P:(g + 1) * P], m[:, h % QR, :],
                                        start=False, stop=(h == H - 1 and m is q_l))
                ins.then_inc(q_used, 1)

            def turn_y(i):
                pe.wait_ge(y0_done, at(i, 1, 1))
                pe.wait_ge(y1_done, at(i, 1, 1))
                pe.wait_ge(added, at(i, 2, 0))
                for j in range(2):
                    for n in range(2):
                        c = 2 * j + n
                        for g in range(KD):
                            ins = pe.transpose(m_bank[1 + 2 * j][:, n * D + g * P:n * D + (g + 1) * P],
                                               yT[:, g, c * P:(c + 1) * P], ident[:, :])
                    ins.then_inc(oT_ready, 1)

            def claim(step):
                before = [n for n in range(step) if prep_banks[n] is prep_banks[step]]
                if before:
                    wait_read(pe, before[-1])
                return prep_bank(step)

            def turn_signs(step, blocks):
                b = claim(step)
                for m, block_m in enumerate(blocks):
                    ins = pe.transpose(b[:, m * P:(m + 1) * P], block_m, ident[:, :])
                ins.then_inc(prep_pe, 1)

            pe.wait_ge(ident_ready, 2)
            pe.wait_ge(w_loaded["v"], 16)
            b = claim(V_STEP)
            for kd in range(KD):
                for n in range(4):
                    ins = pe.transpose(b[:, (4 * kd + n) * R:(4 * kd + n + 1) * R], v_nat[:, kd * P:(kd + 1) * P],
                                       ident[0:R, 0:R])
            ins.then_inc(prep_pe, 1)
            pe.wait_ge(wt_ready, 1)
            b = claim(WT_STEP)
            for kd in range(KD):
                ins = pe.transpose(b[:, kd * P:(kd + 1) * P], wt_nat[:, kd, :], ident[:, :])
            ins.then_inc(prep_pe, 1)
            pe.wait_ge(w_loaded["low"], 16 * 2)
            for n in range(2):
                b = claim(U_STEP + n)
                for m in range(4):
                    ins = pe.transpose(b[0:R, m * P:(m + 1) * P], u_nat[:, 4 * n + m, :], ident[:, :])
                ins.then_inc(prep_pe, 1)
            turn_x(0)
            b = claim(WTB_STEP)
            pe.wait_ge(w_loaded["b"], 16)
            wait_read(pe, WT_STEP)
            for kd in range(KD):
                ins = pe.matmul(b[:, kd * PR:(kd + 1) * PR], wtT[:, kd * P:(kd + 1) * P], b_nat[:, :],
                                start=True, stop=True)
            ins.then_inc(prep_pe, 1)
            pe.wait_ge(split_lo, 3)
            gate_product(0, 0)
            b = claim(LOW_STEP)
            wait_read(pe, U_STEP + 1)
            for h in range(H):
                ins = pe.matmul(b[:, h * R:(h + 1) * R], uT[:, h * P:(h + 1) * P], fb_nat[:, :],
                                start=True, stop=True)
            ins.then_inc(prep_pe, 1)
            pe.wait_ge(uz_split, 1)
            uz_product(0, 0)
            for n in range(4):
                pe.wait_ge(sign1_ready, 4 * (n % 2) + 4)
                turn_signs(T1_STEP + n, [sign1[:, 4 * (n % 2) + m, (n // 2) * P:(n // 2 + 1) * P] for m in range(4)])
            pe.wait_ge(low_ready, 1)
            for n in range(2):
                b = claim(LST_STEP + n)
                for m in range(4):
                    ins = pe.transpose(b[:, m * P:(m + 1) * P], low_rep[:, 4 * n + m, :], ident[:, :])
                ins.then_inc(prep_pe, 1)
            decay_product(0)
            wait_read(pe, LST_STEP + 1)
            pe.wait_ge(zeros_ready, 2)

            def second_layer_weights():
                pe.wait_ge(w_loaded["from"], 16)
                b = claim(WFT_STEP)
                for g in range(KD):
                    ins = pe.transpose(b[:, g * P:(g + 1) * P], wfrom_nat[:, g * P:(g + 1) * P], ident[:, :])
                ins.then_inc(prep_pe, 1)
                pe.wait_ge(wt_split, 1)
                t_product(0, 0)
                pe.wait_ge(sign2_ready, KD)
                for n in range(4):
                    turn_signs(T2_STEP + n, [sign2[:, m % 2, (2 * n + m // 2) * P:(2 * n + m // 2 + 1) * P]
                                             for m in range(4)])
                b = claim(WF_STEP)
                wait_read(pe, WFT_STEP)
                for g in range(KD):
                    ins = pe.transpose(b[:, g * P:(g + 1) * P], wfromT[:, g, :], ident[:, :])
                ins.then_inc(prep_pe, 1)
                c_product(0)

            def tile_steps(i, k):
                first, last = is_tile(i, 0), is_tile(i, NT - 1)
                for h in range(H):
                    hidden(i, k, h)
                    if first and h == 0:
                        second_layer_weights()
                    if not last:
                        if h == 0:
                            turn_x(i + 1)
                        if h == 2:
                            gate_product(i + 1, k + 1)
                        if h == 3:
                            uz_product(i + 1, k + 1)
                        if h == 4:
                            decay_product(i + 1)
                        if h == 6:
                            t_product(i + 1, k + 1)
                        if h == 7:
                            c_product(i + 1)
                    if h == 4 and not first:
                        turn_y(i - 1)
                    if first and h == LAG:
                        wait_read(pe, WF_STEP)
                    if h == LAG:
                        from_product(i)
                    if h >= LAG:
                        project(i, h - LAG)
                    elif not first:
                        project(i - 1, h - LAG + H)

            run_tiles(pe, tile_steps)
            for h in range(H - LAG, H):
                project(NT - 1, h)
            turn_y(NT - 1)


_INS = ["x", "W_toP", "W_U", "W_F", "W_V", "W_lam", "B_mat", "C_mat", "W_fromP"]
_FFN = ["fast_b", "w_fc", "w_proj", "u", "v", "gate"]


def kernel(**inputs):
    import numpy as np
    import concourse.bacc as bacc
    from concourse.bass_utils import run_bass_kernel_spmd

    nc = bacc.Bacc("TRN2", target_bir_lowering=False, num_devices=1)
    arrays, args = {}, []
    for name in [f"L0_attn_{n}" for n in _INS] + [f"L0_ffn_{n}" for n in _FFN]:
        a = np.ascontiguousarray(inputs[name])
        if a.ndim == 0:
            a = a.reshape(1, 1)
        arrays[name] = a
        args.append(nc.dram_tensor(name, a.shape, mybir.dt.from_np(a.dtype), kind="ExternalInput").ap())
    shape = np.asarray(inputs["L0_attn_x"]).shape
    args.append(nc.dram_tensor("out", shape, F32, kind="ExternalOutput").ap())
    build(nc, *args)
    r = run_bass_kernel_spmd(nc, [arrays], core_ids=[0])
    return r.results[0]["out"]
```
